# Optimizing a Trainium2 kernel written in Bass

```python
import numpy as np
import jax
import jax.numpy as jnp

def _softmax(x, axis=-1):
    return jax.nn.softmax(x, axis=axis)

def _gelu(x):
    return jax.nn.gelu(x, approximate=True)

def _silu(x):
    return jax.nn.silu(x)

def _sigmoid(x):
    return jax.nn.sigmoid(x)

def _layernorm(x, axis=-1, eps=1e-05):
    m = jnp.mean(x, axis=axis, keepdims=True)
    v = jnp.var(x, axis=axis, keepdims=True)
    return (x - m) / jnp.sqrt(v + eps)

def _scatter_add(tgt, idx, src, axis=0):
    return tgt.at[idx].add(src)

def _segment_sum(src, seg, n):
    return jax.ops.segment_sum(src, seg, n)
kernel_name = 'mk_vit_tower_d2_tok_img768_r4_90a1f1'

def setup_inputs(seed: int=0):
    np.random.seed(seed)
    _w = jnp.asarray

    def _rec_inputs():
        import jax
        import jax.numpy as jnp
        _rk = jax.random.key(seed)
        x = -0.00016672 + 0.999947 * jax.random.normal(jax.random.fold_in(_rk, 1), (64, 3, 96, 96), jnp.float32)
        return x
    x = _rec_inputs()

    def _L0_tok_setup():
        import jax, jax.numpy as jnp
        import numpy as np
        IMG = 96
        P = 16
        C = 3
        D = 192
        B = 64
        HP = IMG // P
        N = HP * HP
        FD = P * P * C
        key = jax.random.key(seed)
        k1, k2, k3, k4, k5 = jax.random.split(key, 5)
        x = jax.random.normal(k1, (B, C, IMG, IMG), dtype=jnp.float32)
        W = jax.random.normal(k2, (D, FD), dtype=jnp.float32) * 0.02
        b = jax.random.normal(k3, (D,), dtype=jnp.float32) * 0.02
        class_embed = jax.random.normal(k4, (1, 1, D), dtype=jnp.float32) * 0.02
        position_embed = jax.random.normal(k5, (1, 1 + N, D), dtype=jnp.float32) * 0.02
        return {'x': x, 'W': W, 'b': b, 'class_embed': class_embed, 'position_embed': position_embed}
    _L0_tok_all = _L0_tok_setup()
    _L0_tok_in = {k: v for k, v in _L0_tok_all.items() if k in ('W', 'b', 'class_embed', 'position_embed')}
    del _L0_tok_all

    def _L0_attn_setup():
        import jax, jax.numpy as jnp
        import numpy as np
        import math
        D_MODEL = 192
        N_STATES = 16
        D_IN = 2 * D_MODEL
        DT_RANK = math.ceil(D_MODEL / 16)
        KSIZE = 4
        BATCH, SEQ = (2, 256)

        def _mamba_forward(x, W_in, conv_w, conv_b, W_x, W_dt, b_dt, A_log, Dp, W_out):
            b, l, _ = x.shape
            xr = x @ W_in
            xi, res = jnp.split(xr, 2, axis=-1)
            xc = jnp.transpose(xi, (0, 2, 1))
            xc = jax.lax.conv_general_dilated(xc, conv_w, window_strides=(1,), padding=[(KSIZE - 1, 0)], dimension_numbers=('NCH', 'OIH', 'NCH'), feature_group_count=D_IN)
            xc = xc + conv_b[None, :, None]
            xi = jnp.transpose(xc, (0, 2, 1))
            xi = jax.nn.swish(xi)
            A = -jnp.exp(A_log)
            x_dbl = xi @ W_x
            delta, B, C = jnp.split(x_dbl, [DT_RANK, DT_RANK + N_STATES], axis=-1)
            delta = jax.nn.softplus(delta @ W_dt + b_dt)
            dA = jnp.einsum('bld,dn->bldn', delta, A)
            dB_u = jnp.einsum('bld,bld,bln->bldn', delta, xi, B)
            dA_shift = jnp.pad(dA[:, 1:], ((0, 0), (0, 1), (0, 0), (0, 0)))
            dA_cumsum = jnp.exp(jnp.flip(jnp.cumsum(jnp.flip(dA_shift, 1), axis=1), 1))
            x_ss = jnp.cumsum(dB_u * dA_cumsum, axis=1) / (dA_cumsum + 1e-12)
            y = jnp.einsum('bldn,bln->bld', x_ss, C) + xi * Dp
            return y * jax.nn.swish(res) @ W_out
        key = jax.random.key(seed)
        ks = jax.random.split(key, 8)
        s = 0.02
        x = jax.random.normal(ks[0], (BATCH, SEQ, D_MODEL), dtype=jnp.float32)
        W_in = jax.random.normal(ks[1], (D_MODEL, 2 * D_IN), dtype=jnp.float32) * s
        conv_w = jax.random.normal(ks[2], (D_IN, 1, KSIZE), dtype=jnp.float32) * s
        conv_b = jnp.zeros((D_IN,), dtype=jnp.float32)
        W_x = jax.random.normal(ks[3], (D_IN, DT_RANK + 2 * N_STATES), dtype=jnp.float32) * s
        W_dt = jax.random.normal(ks[4], (DT_RANK, D_IN), dtype=jnp.float32) * s
        b_dt = jnp.zeros((D_IN,), dtype=jnp.float32)
        A_log = jnp.log(jnp.broadcast_to(jnp.arange(1, N_STATES + 1, dtype=jnp.float32), (D_IN, N_STATES)))
        Dp = jnp.ones((D_IN,), dtype=jnp.float32)
        W_out = jax.random.normal(ks[5], (D_IN, D_MODEL), dtype=jnp.float32) * s
        return {'x': x, 'W_in': W_in, 'conv_w': conv_w, 'conv_b': conv_b, 'W_x': W_x, 'W_dt': W_dt, 'b_dt': b_dt, 'A_log': A_log, 'Dp': Dp, 'W_out': W_out}
    _L0_attn_all = _L0_attn_setup()
    _L0_attn_in = {k: v for k, v in _L0_attn_all.items() if k in ('W_in', 'conv_w', 'conv_b', 'W_x', 'W_dt', 'b_dt', 'A_log', 'Dp', 'W_out')}
    del _L0_attn_all

    def _L0_ffn_setup():
        import jax, jax.numpy as jnp
        import numpy as np
        B, T, D, E, K = (4, 512, 192, 8, 2)
        H = 4 * D
        key = jax.random.key(seed)
        k0, k1, k2, k3, k4 = jax.random.split(key, 5)
        s = 0.02
        return {'x': jax.random.normal(k0, (B, T, D), jnp.float32), 'router_w': jax.random.uniform(k1, (E, D), jnp.float32, -s * 0.1, s * 0.1), 'Wg': jax.random.uniform(k2, (E, H, D), jnp.float32, -s * 0.4, s * 0.4), 'Wu': jax.random.uniform(k3, (E, H, D), jnp.float32, -s * 0.4, s * 0.4), 'Wd': jax.random.normal(k4, (E, D, H), jnp.float32) * 0.01}
    _L0_ffn_all = _L0_ffn_setup()
    _L0_ffn_in = {k: v for k, v in _L0_ffn_all.items() if k in ('router_w', 'Wg', 'Wu', 'Wd')}
    del _L0_ffn_all

    def _L1_attn_setup():
        import jax, jax.numpy as jnp
        import numpy as np
        DIM = 192
        D_INNER = 384
        D_STATE = 16
        D_CONV = 4
        DT_RANK = 48

        def _mamba(x, W_in, conv_w, conv_b, W_x, W_dt, b_dt, A_log, D, W_out):
            Bb, L, _ = x.shape
            xz = x @ W_in.T
            xp, z = jnp.split(xz, 2, axis=-1)
            xpad = jnp.pad(xp, ((0, 0), (D_CONV - 1, 0), (0, 0)))
            conv = sum((conv_w[:, k] * xpad[:, k:k + L, :] for k in range(D_CONV)))
            xc = jax.nn.silu(conv + conv_b)
            x_dbl = xc @ W_x.T
            dt = x_dbl[..., :DT_RANK]
            Bm = x_dbl[..., DT_RANK:DT_RANK + D_STATE]
            Cm = x_dbl[..., DT_RANK + D_STATE:]
            dt = jax.nn.softplus(dt @ W_dt.T + b_dt)
            A = -jnp.exp(A_log)
            dA = jnp.exp(dt[..., None] * A)
            dBx = (dt * xc)[..., None] * Bm[:, :, None, :]

            def step(h, inp):
                dA_t, dBx_t, C_t = inp
                h = dA_t * h + dBx_t
                return (h, jnp.einsum('bds,bs->bd', h, C_t))
            h0 = jnp.zeros((Bb, D_INNER, D_STATE), x.dtype)
            _, ys = jax.lax.scan(step, h0, (dA.transpose(1, 0, 2, 3), dBx.transpose(1, 0, 2, 3), Cm.transpose(1, 0, 2)))
            y = ys.transpose(1, 0, 2) + xc * D
            y = y * jax.nn.silu(z)
            return y @ W_out.T
        key = jax.random.key(seed)
        ks = jax.random.split(key, 16)

        def nrm(k, shape, s=0.02):
            return jax.random.normal(k, shape, jnp.float32) * s
        d = {'x': jax.random.normal(ks[0], (2, 256, DIM), jnp.float32)}
        A_init = jnp.log(jnp.tile(jnp.arange(1, D_STATE + 1, dtype=jnp.float32), (D_INNER, 1)))
        for i, p in enumerate(['fwd', 'bwd']):
            b = ks[1 + 7 * i:8 + 7 * i]
            d[p + '_W_in'] = nrm(b[0], (2 * D_INNER, DIM))
            d[p + '_conv_w'] = nrm(b[1], (D_INNER, D_CONV), 0.1)
            d[p + '_conv_b'] = jnp.zeros((D_INNER,), jnp.float32)
            d[p + '_W_x'] = nrm(b[2], (DT_RANK + 2 * D_STATE, D_INNER))
            d[p + '_W_dt'] = nrm(b[3], (D_INNER, DT_RANK), 0.1)
            d[p + '_b_dt'] = nrm(b[4], (D_INNER,), 0.1)
            d[p + '_A_log'] = A_init
            d[p + '_D'] = jnp.ones((D_INNER,), jnp.float32)
            d[p + '_W_out'] = nrm(b[5], (DIM, D_INNER))
        return d
    _L1_attn_all = _L1_attn_setup()
    _L1_attn_in = {k: v for k, v in _L1_attn_all.items() if k in ('fwd_W_in', 'fwd_conv_w', 'fwd_conv_b', 'fwd_W_x', 'fwd_W_dt', 'fwd_b_dt', 'fwd_A_log', 'fwd_D', 'fwd_W_out', 'bwd_W_in', 'bwd_conv_w', 'bwd_conv_b', 'bwd_W_x', 'bwd_W_dt', 'bwd_b_dt', 'bwd_A_log', 'bwd_D', 'bwd_W_out')}
    del _L1_attn_all

    def _L1_ffn_setup():
        import jax, jax.numpy as jnp
        import numpy as np
        DEPTH = 11

        def _fff_forward(inputs, weights_in, weights_out, depth=DEPTH):
            B, S, _ = inputs.shape
            n_nodes = weights_in.shape[0]
            max_index = n_nodes - 1
            all_logits = jnp.einsum('bsd,nd->bsn', inputs, weights_in)

            def step(prev_idx, _):
                sel = jnp.clip(prev_idx, 0, max_index)
                logits = jnp.take_along_axis(all_logits, sel[..., None], axis=-1)[..., 0]
                new_idx = jnp.clip(2 * sel + 1 + (logits > 0).astype(sel.dtype), 0, max_index)
                return (new_idx, (logits, new_idx))
            idx0 = jnp.zeros((B, S), dtype=jnp.int32)
            _, (logits_seq, idx_seq) = jax.lax.scan(step, idx0, None, length=depth - 1)
            logits = jnp.concatenate([jnp.zeros((1, B, S), all_logits.dtype), logits_seq], axis=0)
            node_idx = jnp.concatenate([idx0[None], idx_seq], axis=0)
            act = jax.nn.gelu(logits, approximate=False)
            onehot = jax.nn.one_hot(node_idx, n_nodes, dtype=act.dtype)
            coeff = jnp.einsum('dbs,dbsn->bsn', act, onehot)
            return jnp.einsum('bsn,nd->bsd', coeff, weights_out)
        key = jax.random.key(seed)
        k1, k2, k3 = jax.random.split(key, 3)
        B, S, D = (4, 1024, 192)
        n_nodes = 2 * DEPTH - 1
        return {'inputs': jax.random.normal(k1, (B, S, D), dtype=jnp.float32), 'weights_in': jax.random.normal(k2, (n_nodes, D), dtype=jnp.float32), 'weights_out': jax.random.normal(k3, (n_nodes, D), dtype=jnp.float32)}
    _L1_ffn_all = _L1_ffn_setup()
    _L1_ffn_in = {k: v for k, v in _L1_ffn_all.items() if k in ('weights_in', 'weights_out')}
    del _L1_ffn_all
    return {'x': x, 'L0_tok_W': _L0_tok_in['W'], 'L0_tok_b': _L0_tok_in['b'], 'L0_tok_class_embed': _L0_tok_in['class_embed'], 'L0_tok_position_embed': _L0_tok_in['position_embed'], 'L0_attn_W_in': _L0_attn_in['W_in'], 'L0_attn_conv_w': _L0_attn_in['conv_w'], 'L0_attn_conv_b': _L0_attn_in['conv_b'], 'L0_attn_W_x': _L0_attn_in['W_x'], 'L0_attn_W_dt': _L0_attn_in['W_dt'], 'L0_attn_b_dt': _L0_attn_in['b_dt'], 'L0_attn_A_log': _L0_attn_in['A_log'], 'L0_attn_Dp': _L0_attn_in['Dp'], 'L0_attn_W_out': _L0_attn_in['W_out'], 'L0_ffn_router_w': _L0_ffn_in['router_w'], 'L0_ffn_Wg': _L0_ffn_in['Wg'], 'L0_ffn_Wu': _L0_ffn_in['Wu'], 'L0_ffn_Wd': _L0_ffn_in['Wd'], 'L1_attn_fwd_W_in': _L1_attn_in['fwd_W_in'], 'L1_attn_fwd_conv_w': _L1_attn_in['fwd_conv_w'], 'L1_attn_fwd_conv_b': _L1_attn_in['fwd_conv_b'], 'L1_attn_fwd_W_x': _L1_attn_in['fwd_W_x'], 'L1_attn_fwd_W_dt': _L1_attn_in['fwd_W_dt'], 'L1_attn_fwd_b_dt': _L1_attn_in['fwd_b_dt'], 'L1_attn_fwd_A_log': _L1_attn_in['fwd_A_log'], 'L1_attn_fwd_D': _L1_attn_in['fwd_D'], 'L1_attn_fwd_W_out': _L1_attn_in['fwd_W_out'], 'L1_attn_bwd_W_in': _L1_attn_in['bwd_W_in'], 'L1_attn_bwd_conv_w': _L1_attn_in['bwd_conv_w'], 'L1_attn_bwd_conv_b': _L1_attn_in['bwd_conv_b'], 'L1_attn_bwd_W_x': _L1_attn_in['bwd_W_x'], 'L1_attn_bwd_W_dt': _L1_attn_in['bwd_W_dt'], 'L1_attn_bwd_b_dt': _L1_attn_in['bwd_b_dt'], 'L1_attn_bwd_A_log': _L1_attn_in['bwd_A_log'], 'L1_attn_bwd_D': _L1_attn_in['bwd_D'], 'L1_attn_bwd_W_out': _L1_attn_in['bwd_W_out'], 'L1_ffn_weights_in': _L1_ffn_in['weights_in'], 'L1_ffn_weights_out': _L1_ffn_in['weights_out']}

def reference(x, L0_tok_W, L0_tok_b, L0_tok_class_embed, L0_tok_position_embed, L0_attn_W_in, L0_attn_conv_w, L0_attn_conv_b, L0_attn_W_x, L0_attn_W_dt, L0_attn_b_dt, L0_attn_A_log, L0_attn_Dp, L0_attn_W_out, L0_ffn_router_w, L0_ffn_Wg, L0_ffn_Wu, L0_ffn_Wd, L1_attn_fwd_W_in, L1_attn_fwd_conv_w, L1_attn_fwd_conv_b, L1_attn_fwd_W_x, L1_attn_fwd_W_dt, L1_attn_fwd_b_dt, L1_attn_fwd_A_log, L1_attn_fwd_D, L1_attn_fwd_W_out, L1_attn_bwd_W_in, L1_attn_bwd_conv_w, L1_attn_bwd_conv_b, L1_attn_bwd_W_x, L1_attn_bwd_W_dt, L1_attn_bwd_b_dt, L1_attn_bwd_A_log, L1_attn_bwd_D, L1_attn_bwd_W_out, L1_ffn_weights_in, L1_ffn_weights_out):
    import jax
    import jax.numpy as jnp

    def _L0_tok_ref(x, W, b, class_embed, position_embed):
        import jax, jax.numpy as jnp
        import numpy as np
        IMG = 96
        P = 16
        C = 3
        D = 192
        B = 64
        HP = IMG // P
        N = HP * HP
        FD = P * P * C
        Bn = x.shape[0]
        patches = x.reshape(Bn, C, HP, P, HP, P).transpose(0, 2, 4, 1, 3, 5).reshape(Bn, N, FD)
        proj = jnp.einsum('bnf,df->bnd', patches, W) + b
        cls = jnp.broadcast_to(class_embed, (Bn, 1, D))
        out = jnp.concatenate([cls, proj], axis=1) + position_embed
        return out

    def _L0_attn_ref(x, W_in, conv_w, conv_b, W_x, W_dt, b_dt, A_log, Dp, W_out):
        import jax, jax.numpy as jnp
        import numpy as np
        import math
        D_MODEL = 192
        N_STATES = 16
        D_IN = 2 * D_MODEL
        DT_RANK = math.ceil(D_MODEL / 16)
        KSIZE = 4
        BATCH, SEQ = (2, 256)

        def _mamba_forward(x, W_in, conv_w, conv_b, W_x, W_dt, b_dt, A_log, Dp, W_out):
            b, l, _ = x.shape
            xr = x @ W_in
            xi, res = jnp.split(xr, 2, axis=-1)
            xc = jnp.transpose(xi, (0, 2, 1))
            xc = jax.lax.conv_general_dilated(xc, conv_w, window_strides=(1,), padding=[(KSIZE - 1, 0)], dimension_numbers=('NCH', 'OIH', 'NCH'), feature_group_count=D_IN)
            xc = xc + conv_b[None, :, None]
            xi = jnp.transpose(xc, (0, 2, 1))
            xi = jax.nn.swish(xi)
            A = -jnp.exp(A_log)
            x_dbl = xi @ W_x
            delta, B, C = jnp.split(x_dbl, [DT_RANK, DT_RANK + N_STATES], axis=-1)
            delta = jax.nn.softplus(delta @ W_dt + b_dt)
            dA = jnp.einsum('bld,dn->bldn', delta, A)
            dB_u = jnp.einsum('bld,bld,bln->bldn', delta, xi, B)
            dA_shift = jnp.pad(dA[:, 1:], ((0, 0), (0, 1), (0, 0), (0, 0)))
            dA_cumsum = jnp.exp(jnp.flip(jnp.cumsum(jnp.flip(dA_shift, 1), axis=1), 1))
            x_ss = jnp.cumsum(dB_u * dA_cumsum, axis=1) / (dA_cumsum + 1e-12)
            y = jnp.einsum('bldn,bln->bld', x_ss, C) + xi * Dp
            return y * jax.nn.swish(res) @ W_out
        return _mamba_forward(x, W_in, conv_w, conv_b, W_x, W_dt, b_dt, A_log, Dp, W_out)

    def _L0_ffn_ref(x, router_w, Wg, Wu, Wd):
        import jax, jax.numpy as jnp
        import numpy as np
        B, T, D, E, K = (4, 512, 192, 8, 2)
        H = 4 * D
        Bv, Tv, Dv = x.shape
        N = Bv * Tv
        xf = x.reshape(N, Dv)
        logits = (xf @ router_w.T).astype(jnp.float32)
        top_logits, top_idx = jax.lax.top_k(logits, K)
        top_w = jax.nn.softmax(top_logits, axis=-1).astype(x.dtype)
        out = jnp.zeros_like(xf)
        for e in range(E):
            w_e = jnp.sum(top_w * (top_idx == e), axis=-1)
            h = jax.nn.silu(xf @ Wg[e].T) * (xf @ Wu[e].T)
            out = out + h @ Wd[e].T * w_e[:, None]
        return out.reshape(Bv, Tv, Dv)

    def _L1_attn_ref(x, fwd_W_in, fwd_conv_w, fwd_conv_b, fwd_W_x, fwd_W_dt, fwd_b_dt, fwd_A_log, fwd_D, fwd_W_out, bwd_W_in, bwd_conv_w, bwd_conv_b, bwd_W_x, bwd_W_dt, bwd_b_dt, bwd_A_log, bwd_D, bwd_W_out):
        import jax, jax.numpy as jnp
        import numpy as np
        DIM = 192
        D_INNER = 384
        D_STATE = 16
        D_CONV = 4
        DT_RANK = 48

        def _mamba(x, W_in, conv_w, conv_b, W_x, W_dt, b_dt, A_log, D, W_out):
            Bb, L, _ = x.shape
            xz = x @ W_in.T
            xp, z = jnp.split(xz, 2, axis=-1)
            xpad = jnp.pad(xp, ((0, 0), (D_CONV - 1, 0), (0, 0)))
            conv = sum((conv_w[:, k] * xpad[:, k:k + L, :] for k in range(D_CONV)))
            xc = jax.nn.silu(conv + conv_b)
            x_dbl = xc @ W_x.T
            dt = x_dbl[..., :DT_RANK]
            Bm = x_dbl[..., DT_RANK:DT_RANK + D_STATE]
            Cm = x_dbl[..., DT_RANK + D_STATE:]
            dt = jax.nn.softplus(dt @ W_dt.T + b_dt)
            A = -jnp.exp(A_log)
            dA = jnp.exp(dt[..., None] * A)
            dBx = (dt * xc)[..., None] * Bm[:, :, None, :]

            def step(h, inp):
                dA_t, dBx_t, C_t = inp
                h = dA_t * h + dBx_t
                return (h, jnp.einsum('bds,bs->bd', h, C_t))
            h0 = jnp.zeros((Bb, D_INNER, D_STATE), x.dtype)
            _, ys = jax.lax.scan(step, h0, (dA.transpose(1, 0, 2, 3), dBx.transpose(1, 0, 2, 3), Cm.transpose(1, 0, 2)))
            y = ys.transpose(1, 0, 2) + xc * D
            y = y * jax.nn.silu(z)
            return y @ W_out.T
        fw = _mamba(x, fwd_W_in, fwd_conv_w, fwd_conv_b, fwd_W_x, fwd_W_dt, fwd_b_dt, fwd_A_log, fwd_D, fwd_W_out)
        bw = _mamba(jnp.flip(x, 1), bwd_W_in, bwd_conv_w, bwd_conv_b, bwd_W_x, bwd_W_dt, bwd_b_dt, bwd_A_log, bwd_D, bwd_W_out)
        return fw + jnp.flip(bw, 1) + x

    def _L1_ffn_ref(inputs, weights_in, weights_out):
        import jax, jax.numpy as jnp
        import numpy as np
        DEPTH = 11

        def _fff_forward(inputs, weights_in, weights_out, depth=DEPTH):
            B, S, _ = inputs.shape
            n_nodes = weights_in.shape[0]
            max_index = n_nodes - 1
            all_logits = jnp.einsum('bsd,nd->bsn', inputs, weights_in)

            def step(prev_idx, _):
                sel = jnp.clip(prev_idx, 0, max_index)
                logits = jnp.take_along_axis(all_logits, sel[..., None], axis=-1)[..., 0]
                new_idx = jnp.clip(2 * sel + 1 + (logits > 0).astype(sel.dtype), 0, max_index)
                return (new_idx, (logits, new_idx))
            idx0 = jnp.zeros((B, S), dtype=jnp.int32)
            _, (logits_seq, idx_seq) = jax.lax.scan(step, idx0, None, length=depth - 1)
            logits = jnp.concatenate([jnp.zeros((1, B, S), all_logits.dtype), logits_seq], axis=0)
            node_idx = jnp.concatenate([idx0[None], idx_seq], axis=0)
            act = jax.nn.gelu(logits, approximate=False)
            onehot = jax.nn.one_hot(node_idx, n_nodes, dtype=act.dtype)
            coeff = jnp.einsum('dbs,dbsn->bsn', act, onehot)
            return jnp.einsum('bsn,nd->bsd', coeff, weights_out)
        return _fff_forward(inputs, weights_in, weights_out)
    h = _L0_tok_ref(x, L0_tok_W, L0_tok_b, L0_tok_class_embed, L0_tok_position_embed)
    h = h + _L0_attn_ref(_layernorm(h, axis=-1), L0_attn_W_in, L0_attn_conv_w, L0_attn_conv_b, L0_attn_W_x, L0_attn_W_dt, L0_attn_b_dt, L0_attn_A_log, L0_attn_Dp, L0_attn_W_out)
    h = h + _L0_ffn_ref(_layernorm(h, axis=-1), L0_ffn_router_w, L0_ffn_Wg, L0_ffn_Wu, L0_ffn_Wd)
    h = h + _L1_attn_ref(_layernorm(h, axis=-1), L1_attn_fwd_W_in, L1_attn_fwd_conv_w, L1_attn_fwd_conv_b, L1_attn_fwd_W_x, L1_attn_fwd_W_dt, L1_attn_fwd_b_dt, L1_attn_fwd_A_log, L1_attn_fwd_D, L1_attn_fwd_W_out, L1_attn_bwd_W_in, L1_attn_bwd_conv_w, L1_attn_bwd_conv_b, L1_attn_bwd_W_x, L1_attn_bwd_W_dt, L1_attn_bwd_b_dt, L1_attn_bwd_A_log, L1_attn_bwd_D, L1_attn_bwd_W_out)
    h = h + _L1_ffn_ref(_layernorm(h, axis=-1), L1_ffn_weights_in, L1_ffn_weights_out)
    return h

_drawn_inputs = setup_inputs


def setup_inputs(seed=0):
    import zlib

    import numpy as np

    out = dict(_drawn_inputs(seed))
    spreads = {'L0_attn_conv_b': (0.0, 0.1),
     'L0_attn_b_dt': (0.0, 2.0),
     'L0_attn_Dp': (1.0, 0.6),
     'L1_attn_fwd_conv_b': (0.0, 0.444),
     'L1_attn_fwd_D': (1.0, 0.6),
     'L1_attn_bwd_conv_b': (0.0, 0.491),
     'L1_attn_bwd_D': (1.0, 0.6)}
    factors = {'L0_attn_conv_w': 7.402,
     'L0_attn_W_x': 64.0,
     'L0_attn_W_dt': 64.0,
     'L0_attn_A_log': 64.0,
     'L0_ffn_router_w': 7.878,
     'L0_ffn_Wg': 8.0,
     'L0_ffn_Wu': 7.231,
     'L0_ffn_Wd': 8.0,
     'L1_attn_fwd_W_in': 3.301,
     'L1_attn_fwd_conv_w': 8.0,
     'L1_attn_fwd_W_x': 8.0,
     'L1_attn_fwd_W_dt': 8.0,
     'L1_attn_fwd_b_dt': 38.696,
     'L1_attn_fwd_A_log': 8.0,
     'L1_attn_fwd_W_out': 3.703,
     'L1_attn_bwd_W_in': 4.39,
     'L1_attn_bwd_conv_w': 7.264,
     'L1_attn_bwd_W_x': 8.0,
     'L1_attn_bwd_W_dt': 8.0,
     'L1_attn_bwd_b_dt': 8.0,
     'L1_attn_bwd_A_log': 8.0,
     'L1_attn_bwd_W_out': 5.211}
    for name, (base, spread) in spreads.items():
        noise = np.random.default_rng([zlib.crc32(name.encode()), seed]).standard_normal(out[name].shape)
        drawn = base * np.exp(spread * noise) if base else spread * noise
        out[name] = jnp.asarray(drawn.astype(out[name].dtype))
    for name, factor in factors.items():
        out[name] = (out[name] * factor).astype(out[name].dtype)
    return out
```

```python
from contextlib import ExitStack

import numpy as np

import concourse.bass as bass
from concourse import mybir

F32 = mybir.dt.float32
BF16 = mybir.dt.bfloat16
ALU = mybir.AluOpType
ACT = mybir.ActivationFunctionType
AX_X = mybir.AxisListType.X

IMAGES, SIDE, PATCH, COLORS = 64, 96, 16, 3
GRID = SIDE // PATCH
PATCHES = GRID * GRID
SEQ = PATCHES + 1
TOKENS = IMAGES * SEQ
D = 192
DP = D // 2
DH = 2
PIXELS = PATCH * PATCH * COLORS
PK = PIXELS // 128
INNER = 2 * D
J = INNER // 128
STATES = 16
TAPS = 4
BC = 2 * STATES
EXPERTS = 8
HID = 4 * D
HK = HID // 128
NODES = 21
FFF_STEPS = 10
EPS_LN = 1e-5
EPS_SCAN = 1e-12
LOG_RATE_MAX = 80.0

CI = 8
CHUNKS = IMAGES // CI
CT = CI * SEQ
CPATCH = CI * PATCHES
TG = 4
TP = CT // TG
GROUPS = CHUNKS * TG
NG = 4
NS = STATES // NG
GROUP_COLS = NS * J * CT
BANK = 512

V_CONV, V_CONVB, V_DTB, V_SKIP, V_ALOG = 0, J * TAPS, J * TAPS + J, J * TAPS + 2 * J, J * TAPS + 3 * J
V_COLS = V_ALOG + J * STATES


def imgs(ap):
    return ap.rearrange("p (i t) -> p i t", t=SEQ)


class MambaWeights:

    def __init__(self, sb, name, rank, ratio, rev):
        self.name, self.rank, self.ratio, self.rev = name, rank, ratio, rev
        self.w_in = sb(f"{name}_w_in", [DP, DH, 2 * INNER], F32)
        self.w_x = sb(f"{name}_w_x", [128, J, rank + 3 * BC], F32)
        self.w_dt = sb(f"{name}_w_dt", [rank, INNER], F32)
        self.w_out = sb(f"{name}_w_out", [128, J, D], F32)
        self.vec = sb(f"{name}_vec", [128, V_COLS], F32)
        self.a = sb(f"{name}_a", [128, J * STATES], F32)
        self.xpad = sb(f"{name}_xpad", [128, J, CI, SEQ + TAPS - 1], F32)
        self.decay = [sb(f"{name}_decay{i}", [128, NS, J, CT], F32) for i in range(2)]

    def conv_w(self, j, k):
        at = V_CONV + j * TAPS + k
        return self.vec[:, at:at + 1]

    def col(self, at, j):
        return self.vec[:, at + j:at + j + 1]

    def load(self, sp, drams, done):
        for tile, dram in zip((self.w_in, self.w_x, self.w_dt, self.w_out, self.vec), drams):
            full = (slice(None),) * len(tile.shape)
            sp.dma_start(tile[full], dram).then_inc(done, 16)


def build(nc, t):
    with ExitStack() as whole:
        def keep(name, shape, dt):
            return whole.enter_context(nc.sbuf_tensor(name, shape, dt))

        h_all = keep("h_all", [DP, DH, TOKENS], F32)
        node_all = keep("node_all", [TP, GROUPS, NODES], F32)
        ident = keep("ident", [128, 128], F32)
        rep32 = keep("rep32", [3 * BC, BC], F32)
        sel = keep("sel", [3 * BC, BC, 128], BF16)
        mean_w = keep("mean_w", [DP, DP], F32)
        eps_ln = keep("eps_ln", [128, 1], F32)
        eps_scan = keep("eps_scan", [128, 1], F32)
        one = keep("one", [128, 1], F32)

        with (
            nc.sbuf_tensor("route_all", [TP, GROUPS, EXPERTS], F32) as route_all,
        ):
            mamba_phase(nc, t, first=True, h_all=h_all, z_all=None, logits_all=route_all, ident=ident, rep32=rep32,
                        sel=sel, mean_w=mean_w, eps_ln=eps_ln, eps_scan=eps_scan, one=one)
            expert_phase(nc, t, h_all, route_all, ident, sel)
        mamba_phase(nc, t, first=False, h_all=h_all, z_all=None, logits_all=node_all, ident=ident, rep32=rep32,
                    sel=sel, mean_w=mean_w, eps_ln=eps_ln, eps_scan=eps_scan, one=one)
        tree_phase(nc, t, h_all, node_all, ident)


def since(eng, sem, n):
    if not isinstance(n, int) or n > 0:
        eng.wait_ge(sem, n)


def mamba_phase(nc, t, first, h_all, z_all, logits_all, ident, rep32, sel, mean_w, eps_ln, eps_scan, one):
    tag = "a" if first else "c"
    LOGITS = EXPERTS if first else NODES
    with ExitStack() as ctx:
        def sb(name, shape, dt):
            return ctx.enter_context(nc.sbuf_tensor(f"{tag}_{name}", shape, dt))

        def pb(name, shape, dt):
            return ctx.enter_context(nc.psum_tensor(f"{tag}_{name}", shape, dt))

        def sem(name):
            return ctx.enter_context(nc.semaphore(f"{tag}_{name}"))

        if first:
            blocks = [MambaWeights(sb, "m0", 12, True, False)]
            loads = [t["m0"]]
        else:
            blocks = [MambaWeights(sb, "mf", 48, False, False), MambaWeights(sb, "mb", 48, False, True)]
            loads = [t["mf"], t["mb"]]
        NB = len(blocks)
        UNITS = NB * CHUNKS

        w_logit = sb("w_logit", [DP, DH, LOGITS], F32)
        hc = sb("hc", [DP, DH, CT], F32)
        rank_max = max(b.rank for b in blocks)
        gate = [sb(f"gate{i}", [128, J, CT], F32) for i in range(2)]
        xc = [sb(f"xc{i}", [128, J, CT], F32) for i in range(2)]
        parts = [sb(f"parts{i}", [3 * BC, CT], BF16) for i in range(2)]
        conv = sb("conv", [128, J, CT], F32)
        dtr = sb("dtr", [rank_max, CT], F32)
        bc = sb("bc", [3 * BC, CT], F32)
        bcr = sb("bcr", [3 * BC, CT], F32)
        absx = sb("absx", [128, J, CT], F32)
        relux = sb("relux", [128, J, CT], F32)
        lnx = sb("lnx", [128, J, CT], F32)
        delta = sb("delta", [128, J, CT], F32)
        dx = sb("dx", [128, J, CT], F32)
        val = [sb(f"val{i}", [128, NS, J, CT], F32) for i in range(2)]
        y = sb("y", [128, J, CT], F32)
        if first:
            w_tok = sb("w_tok", [128, PK, D], F32)
            xin = sb("xin", [128, PK, CPATCH], F32)
            pos = sb("pos", [DP, DH, SEQ], F32)
            clsb = sb("clsb", [DP, DH, 2], F32)
            posb = sb("posb", [DP, DH, SEQ], F32)
            keep_fwd = sb("keep_fwd", [128, NS * J * CI, SEQ], BF16)
            keep_bwd = sb("keep_bwd", [128, J * CI, SEQ], BF16)
            suffix = sb("suffix", [128, J, CT], F32)
            inv = sb("inv", [128, NS, J, CT], F32)

        ps = pb("ps", [128, 3, BANK], F32)
        ps_y = pb("ps_y", [128, J, BANK], F32)
        ps_bc = pb("ps_bc", [128, 2, BANK], F32)

        class Norm:

            def __init__(self, name):
                self.cent = sb(f"{name}_cent", [DP, DH, CT], F32)
                self.sq = sb(f"{name}_sq", [DP, DH, CT], F32)
                self.rstd = sb(f"{name}_rstd", [DP, CT], F32)
                self.z = sb(f"{name}_z", [DP, DH, CT], F32)
                self.s_mean = sem(f"{name}_s_mean")
                self.s_cent = sem(f"{name}_s_cent")
                self.s_sq = sem(f"{name}_s_sq")
                self.s_var = sem(f"{name}_s_var")
                self.s_rstd = sem(f"{name}_s_rstd")
                self.s_z = sem(f"{name}_s_z")

        before, behind = Norm("before"), Norm("behind")

        s_load = sem("s_load")
        s_set = sem("s_set")
        s_alog = sem("s_alog")
        s_seta = sem("s_seta")
        s_zero = sem("s_zero")
        s_x = sem("s_x")
        s_tok = sem("s_tok")
        s_tokh = sem("s_tokh")
        s_hc = sem("s_hc")
        s_logit = sem("s_logit")
        s_chunk = sem("s_chunk")
        s_zst = sem("s_zst")
        s_xi = sem("s_xi")
        s_xpad = sem("s_xpad")
        s_gp = sem("s_gp")
        s_gate = sem("s_gate")
        s_conv = sem("s_conv")
        s_xc = sem("s_xc")
        s_dbl = sem("s_dbl")
        s_dblc = sem("s_dblc")
        s_parts = sem("s_parts")
        s_dtp = sem("s_dtp")
        s_abs = sem("s_abs")
        s_exp = sem("s_exp")
        s_low = sem("s_low")
        s_delta = sem("s_delta")
        s_suf = sem("s_suf")
        s_dx = sem("s_dx")
        s_bc = sem("s_bc")
        s_v = sem("s_v")
        s_dec = sem("s_dec")
        s_ve = sem("s_ve")
        s_inv = sem("s_inv")
        s_scan = sem("s_scan")
        s_vr = sem("s_vr")
        s_hcm = sem("s_hcm")
        s_sum = sem("s_sum")
        s_skip = sem("s_skip")
        s_y = sem("s_y")
        s_out = sem("s_out")

        block = ctx.enter_context(nc.Block())
        N_SETV = 8 if first else 0
        N_LOAD = 5 * NB + (6 if first else 1)
        N_ZERO = 7 if first else 3 * NB
        HC_PER = 1 if first else 3


        class Unit:

            def __init__(self, u, even, half):
                self.u = u
                self.buf = 0 if even else 1
                self.b = blocks[0] if first or even else blocks[1]
                self.c = u if first else half
                self.opens = first or even
                self.ends = first or not even
                self.g = u * NG

        def units(eng, run):
            run.front(Unit(0, True, 0))
            run.main(Unit(0, True, 0), None, Unit(1, False, 0))
            with eng.Fori(0, UNITS // 2 - 1) as i:
                a, o, e, n = (Unit(i * 2, True, i), Unit(i * 2 + 1, False, i), Unit(i * 2 + 2, True, i + 1),
                              Unit(i * 2 + 3, False, i + 1))
                run.main(o, a, e)
                run.main(e, o, n)
            end = UNITS - 1
            run.main(Unit(end, False, end // 2), Unit(end - 1, True, end // 2), None)
            run.last(Unit(end, False, end // 2))

        def b_row(g, n):
            return n if g == 0 else NS + 2 * NS * (g - 1) + n

        def c_row(g, n):
            return (NS + 2 * NS * g + NS if g < NG - 1 else 2 * STATES - NS) + n

        ROWS = {}
        for g_ in range(NG):
            for n_ in range(NS):
                ROWS[b_row(g_, n_)] = (s_v, g_ * NS + n_ + 1)
                ROWS[c_row(g_, n_)] = (s_hcm, g_ * NS + n_ + 1)

        @block.sync
        def _(sp):
            if first:
                sp.dma_start(ident[:, :], t["ident"]).then_inc(s_load, 16)
                sp.dma_start(rep32[:, :], t["rep32"]).then_inc(s_load, 16)
                sp.dma_start(w_tok[:, :, :], t["w_tok"]).then_inc(s_load, 16)
                sp.dma_start(pos[:, :, :], t["pos"]).then_inc(s_load, 16)
                sp.dma_start(clsb[:, :, :], t["clsb"]).then_inc(s_load, 16)
                sp.dma_start(xin[:, :, :], t["x"][0]).then_inc(s_x, 16)
            sp.dma_start(w_logit[:, :, :], t["router"] if first else t["node_in"]).then_inc(s_load, 16)
            for b, drams in zip(blocks, loads):
                b.load(sp, drams, s_load)
            if first:

                def load(c):
                    sp.wait_ge(s_tok, c)
                    sp.dma_start(xin[:, :, :], t["x"][c]).then_inc(s_x, 16)

                def store(c):
                    sp.wait_ge(behind.s_z, c + 1)
                    sp.dma_start(t["z_scratch"][:, :, bass.ds(c * CT, CT)], behind.z[:, :, :]).then_inc(s_zst, 16)

                load(1)
                with sp.Fori(2, CHUNKS) as c:
                    load(c)
                    store(c - 2)
                store(CHUNKS - 2)
                store(CHUNKS - 1)
                sp.wait_ge(s_zst, 16 * CHUNKS)

        @block.gpsimd
        def _(pool):
            g = nc.gpsimd
            for b in blocks:
                edge = b.xpad[:, :, :, SEQ:] if b.rev else b.xpad[:, :, :, 0:TAPS - 1]
                g.memset(edge, 0.0).then_inc(s_zero, 1)
                for i in range(2):
                    at = SEQ - 1 if (b.rev or b.ratio) else 0
                    col = b.decay[i][:, :, :, :].rearrange("p n j (i t) -> p (n j i) t", t=SEQ)[:, :, at:at + 1]
                    g.memset(col, 1.0 if b.ratio else 0.0).then_inc(s_zero, 1)
            if first:
                g.memset(keep_fwd[:, :, :], 1.0).then_inc(s_zero, 1)
                g.memset(keep_bwd[:, :, :], 1.0).then_inc(s_zero, 1)
                pool.wait_ge(s_zero, 5)
                g.memset(keep_fwd[:, :, 0:1], 0.0).then_inc(s_zero, 1)
                g.memset(keep_bwd[:, :, SEQ - 1:SEQ], 0.0).then_inc(s_zero, 1)
                with pool.Fori(0, UNITS) as u:
                    for gi in range(NG):
                        pool.wait_ge(s_dec, (u * NG + gi + 1) * (NS * J))
                        pool.wait_ge(s_v, u * STATES + NS * (gi + 1))
                        v = val[gi % 2][:, :, :, :].rearrange("p n j t -> p (n j t)")
                        e = blocks[0].decay[gi % 2][:, :, :, :].rearrange("p n j t -> p (n j t)")
                        g.tensor_tensor(v, v, e, ALU.mult).then_inc(s_ve, 1)

        @block.tensor
        def _(pe):
            mm = nc.tensor.matmul
            pe.wait_ge(s_load, 16 * N_LOAD)
            since(pe, s_set, N_SETV)

            def statistic(src, bank, done):
                for k in range(DH):
                    m = mm(ps[0:DP, bank, 0:CT], mean_w[:, :], src(k), start=(k == 0), stop=(k == DH - 1))
                m.then_inc(done, 1)

            def row(x, idx, n):
                if idx >= 2:
                    used, count = ROWS[idx - 2]
                    pe.wait_ge(used, x.u * STATES + count)
                else:
                    since(pe, s_hcm, x.u * STATES - 1 + idx)
                if idx == 0:
                    pe.wait_ge(s_parts, x.u * 5 + 5)
                mm(ps_bc[:, idx % 2, 0:CT], sel[:, n, :], parts[x.buf][:, :], start=True, stop=True).then_inc(s_bc, 1)

            def b_rows(x, gi, ns=range(NS)):
                for n in ns:
                    row(x, b_row(gi, n), gi * NS + n)

            def c_rows(x, gi, ns):
                for n in ns:
                    row(x, c_row(gi, n), STATES + gi * NS + n)

            def add_up(x, gi, n):
                s = gi * NS + n
                if s == 0:
                    since(pe, s_skip, x.u * J)
                pe.wait_ge(s_hcm, x.u * STATES + s + 1)
                for j in range(J):
                    m = mm(ps_y[:, j, 0:CT], ident[:, :], val[gi % 2][:, n, j, :], start=(s == 0), stop=(s == STATES - 1))
                if n == NS - 1:
                    m.then_inc(s_sum, 1)

            def f_tok(x):
                if not first:
                    return
                pe.wait_ge(s_x, x.c * 16 + 16)
                since(pe, s_chunk, 2 * (x.c - 1))
                since(pe, s_abs, x.u * (2 * J))
                for m_ in range(DH):
                    for k in range(PK):
                        m = mm(ps[0:DP, m_, 0:CPATCH], w_tok[:, k, m_ * DP:(m_ + 1) * DP], xin[:, k, :],
                               start=(k == 0), stop=(k == PK - 1))
                m.then_inc(s_tok, 1)

            def f_mean(x):
                if x.opens:
                    if first:
                        pe.wait_ge(s_tokh, x.c * 3 + 3)
                    else:
                        since(pe, s_hc, (x.c - 1) * HC_PER + 2)
                        since(pe, s_abs, x.u * (2 * J))
                    statistic(lambda k: h_all[:, k, bass.ds(x.c * CT, CT)], 0, before.s_mean)

            def f_var(x):
                if x.opens:
                    pe.wait_ge(before.s_sq, x.c + 1)
                    statistic(lambda k: before.sq[:, k, :], 1, before.s_var)

            def project_in(x, half, ready):
                for j in range(J):
                    for k in range(DH):
                        at = half * INNER + j * 128
                        m = mm(ps[:, j, 0:CT], x.b.w_in[:, k, at:at + 128], before.z[:, k, :],
                               start=(k == 0), stop=(k == DH - 1))
                m.then_inc(ready, 1)

            def f_xi(x):
                pe.wait_ge(before.s_z, x.c + 1)
                if not x.opens:
                    since(pe, s_chunk, x.c * 2)
                    pe.wait_ge(s_abs, x.u * (2 * J))
                project_in(x, 0, s_xi)

            def f_gate(x):
                pe.wait_ge(s_xpad, x.u + 1)
                project_in(x, 1, s_gp)

            def f_dbl(x):
                pe.wait_ge(s_gate, x.u + 1)
                pe.wait_ge(s_xc, x.u * J + J)
                r = x.b.rank
                for j in range(J):
                    mm(ps[0:r, 0, 0:CT], x.b.w_x[:, j, 0:r], xc[x.buf][:, j, :], start=(j == 0), stop=(j == J - 1))
                for j in range(J):
                    m = mm(ps[0:3 * BC, 1, 0:CT], x.b.w_x[:, j, r:r + 3 * BC], xc[x.buf][:, j, :],
                           start=(j == 0), stop=(j == J - 1))
                m.then_inc(s_dbl, 1)

            def f_dt(x):
                pe.wait_ge(s_dblc, x.u * 3 + 2)
                for j in range(J):
                    m = mm(ps[:, j, 0:CT], x.b.w_dt[:, j * 128:(j + 1) * 128], dtr[0:x.b.rank, :], start=True, stop=True)
                m.then_inc(s_dtp, 1)

            def t_out(x):
                pe.wait_ge(s_y, x.u + 1)
                pe.wait_ge(s_abs, (x.u + 1 + (0 if isinstance(x.u, int) and x.u == UNITS - 1 else 1)) * (2 * J))
                for m_ in range(DH):
                    for j in range(J):
                        m = mm(ps[0:DP, m_, 0:CT], x.b.w_out[:, j, m_ * DP:(m_ + 1) * DP], y[:, j, :],
                               start=(j == 0), stop=(j == J - 1))
                m.then_inc(s_out, 1)

            def t_mean(x):
                if x.ends:
                    pe.wait_ge(s_hc, x.c * HC_PER + HC_PER)
                    statistic(lambda k: hc[:, k, :], 0, behind.s_mean)

            def t_var(x):
                if x.ends:
                    pe.wait_ge(behind.s_sq, x.c + 1)
                    statistic(lambda k: behind.sq[:, k, :], 1, behind.s_var)

            def t_logits(x):
                if not x.ends:
                    return
                pe.wait_ge(behind.s_z, x.c + 1)
                for q in range(TG):
                    for k in range(DH):
                        m = mm(ps[0:TP, 2, q * LOGITS:(q + 1) * LOGITS], behind.z[:, k, q * TP:(q + 1) * TP],
                               w_logit[:, k, :], start=(k == 0), stop=(k == DH - 1))
                m.then_inc(s_logit, 1)

            class Run:
                def front(self, f):
                    for step in (f_tok, f_mean, f_var, f_xi, f_gate, f_dbl, f_dt):
                        step(f)

                def main(self, x, tail, front):
                    def do(step, unit):
                        if unit is not None:
                            step(unit)

                    b_rows(x, 0)
                    b_rows(x, 1)
                    do(t_out, tail)
                    c_rows(x, 0, range(2))
                    do(t_mean, tail)
                    c_rows(x, 0, range(2, NS))
                    do(t_var, tail)
                    for n in range(NS):
                        add_up(x, 0, n)
                    do(t_logits, tail)
                    b_rows(x, 2)
                    c_rows(x, 1, range(2))
                    do(f_tok, front)
                    do(f_mean, front)
                    c_rows(x, 1, range(2, NS))
                    do(f_var, front)
                    add_up(x, 1, 0)
                    add_up(x, 1, 1)
                    b_rows(x, 3, range(2))
                    add_up(x, 1, 2)
                    add_up(x, 1, 3)
                    b_rows(x, 3, range(2, NS))
                    c_rows(x, 2, range(2))
                    do(f_xi, front)
                    do(f_gate, front)
                    c_rows(x, 2, range(2, NS))
                    add_up(x, 2, 0)
                    c_rows(x, 3, range(2))
                    do(f_dbl, front)
                    add_up(x, 2, 1)
                    add_up(x, 2, 2)
                    add_up(x, 2, 3)
                    c_rows(x, 3, range(2, NS))
                    do(f_dt, front)
                    for n in range(NS):
                        add_up(x, 3, n)

                def last(self, x):
                    for step in (t_out, t_mean, t_var, t_logits):
                        step(x)

            units(pe, Run())

        @block.scalar
        def _(act):
            a = nc.scalar.activation
            act.wait_ge(s_load, 16 * N_LOAD)
            act.wait_ge(s_alog, NB)
            use_set = nc.scalar.preload_act_table_set
            use_set("natural_log_exp_and_others")
            for b in blocks:
                a(b.a[:, :], b.a[:, :], ACT.Exp).then_inc(s_seta, 1)
            act.wait_ge(s_zero, N_ZERO)
            since(act, s_set, N_SETV)

            def norm(n, c):
                act.wait_ge(n.s_cent, c + 1)
                a(n.sq[:, :, :], n.cent[:, :, :], ACT.Square).then_inc(n.s_sq, 1)
                act.wait_ge(n.s_var, c + 1)
                a(n.rstd[:, :], ps[0:DP, 1, 0:CT], ACT.Ln, bias=eps_ln[0:DP, :]).then_inc(n.s_rstd, 1)
                act.wait_ge(n.s_rstd, c * 2 + 1)
                a(n.rstd[:, :], n.rstd[:, :], ACT.Exp, scale=-0.5).then_inc(n.s_rstd, 1)

            def f_norm(x):
                if x.opens:
                    norm(before, x.c)

            def t_norm(x):
                if x.ends:
                    norm(behind, x.c)

            def f_xpad(x):
                b = x.b
                act.wait_ge(s_xi, x.u + 1)
                inside = b.xpad[:, :, :, 0:SEQ] if b.rev else b.xpad[:, :, :, TAPS - 1:]
                a(inside, ps[:, :, 0:CT].rearrange("p j (i t) -> p j i t", t=SEQ), ACT.Copy).then_inc(s_xpad, 1)
                act.wait_ge(s_gp, x.u + 1)
                since(act, s_y, x.u - 1)
                a(gate[x.buf][:, :, :], ps[:, :, 0:CT], ACT.Silu).then_inc(s_gate, 1)

            def f_xc(x):
                for j in range(J):
                    act.wait_ge(s_conv, x.u * TAPS * J + (TAPS - 1) * J + j + 1)
                    a(xc[x.buf][:, j, :], conv[:, j, :], ACT.Silu, bias=x.b.col(V_CONVB, j)).then_inc(s_xc, 1)
                use_set("natural_log_exp_and_others")

            def f_dbl(x):
                r = x.b.rank
                act.wait_ge(s_dbl, x.u + 1)
                a(dtr[0:r, :], ps[0:r, 0, 0:CT], ACT.Copy).then_inc(s_dblc, 1)
                a(bc[:, :], ps[0:3 * BC, 1, 0:CT], ACT.Copy).then_inc(s_dblc, 1)
                act.wait_ge(s_dblc, x.u * 3 + 2)
                a(parts[x.buf][:, :], bc[:, :], ACT.Copy).then_inc(s_dblc, 1)

            def f_soft(x):
                act.wait_ge(s_dtp, x.u + 1)
                for j in range(J):
                    a(absx[:, j, :], ps[:, j, 0:CT], ACT.Abs, bias=x.b.col(V_DTB, j)).then_inc(s_abs, 1)
                for j in range(J):
                    a(relux[:, j, :], ps[:, j, 0:CT], ACT.Relu, bias=x.b.col(V_DTB, j)).then_inc(s_abs, 1)
                act.wait_ge(s_abs, x.u * 2 * J + J)
                a(absx[:, :, :], absx[:, :, :], ACT.Exp, scale=-1.0).then_inc(s_exp, 1)
                use_set("natural_log")
                act.wait_ge(s_exp, x.u * 2 + 1)
                a(lnx[:, :, :], absx[:, :, :], ACT.Ln, bias=one[:, :]).then_inc(s_exp, 1)
                use_set("natural_log_exp_and_others")

            def decay(x, gi):
                b = x.b
                if gi == 0 and b is blocks[0]:
                    act.wait_ge(s_seta, NB * 2)
                if b.ratio:
                    act.wait_ge(s_suf, x.u + 1)
                    src, lo, hi, take = suffix, 0, SEQ - 1, slice(1, SEQ)
                else:
                    act.wait_ge(s_delta, x.u * 2 + 2)
                    src = delta
                    lo, hi = (0, SEQ - 1) if b.rev else (1, SEQ)
                    take = slice(lo, hi)
                if first or gi >= 2:
                    since(act, s_scan, x.g + gi - 1)
                if b.ratio:
                    since(act, s_inv, (x.g + gi - 1) * 2)
                e = b.decay[gi % 2]
                for n in range(NS):
                    for j in range(J):
                        at = j * STATES + gi * NS + n
                        a(imgs(e[:, n, j, :])[:, :, lo:hi], imgs(src[:, j, :])[:, :, take], ACT.Exp,
                          scale=b.a[:, at:at + 1]).then_inc(s_dec, 1)

            def inverse(x, gi):
                if not x.b.ratio:
                    return
                e = x.b.decay[gi % 2]
                act.wait_ge(s_dec, (x.g + gi + 1) * (NS * J))
                since(act, s_vr, x.g + gi)
                a(inv[:, :, :, :], e[:, :, :, :], ACT.Ln, bias=eps_scan[:, :]).then_inc(s_inv, 1)
                act.wait_ge(s_inv, (x.g + gi) * 2 + 1)
                a(inv[:, :, :, :], inv[:, :, :, :], ACT.Exp, scale=-1.0).then_inc(s_inv, 1)

            def first_groups(x):
                decay(x, 0)
                inverse(x, 0)
                decay(x, 1)

            class Run:
                def front(self, f):
                    for step in (f_norm, f_xpad, f_xc, f_dbl, f_soft, first_groups):
                        step(f)

                def main(self, x, tail, front):
                    if tail is not None:
                        t_norm(tail)
                    inverse(x, 1)
                    decay(x, 2)
                    if front is not None:
                        f_norm(front)
                    inverse(x, 2)
                    decay(x, 3)
                    if front is not None:
                        f_xpad(front)
                        f_xc(front)
                    inverse(x, 3)
                    if front is not None:
                        f_dbl(front)
                        f_soft(front)
                        first_groups(front)

                def last(self, x):
                    t_norm(x)

            units(act, Run())

        @block.vector
        def _(dve):
            v_ = nc.vector
            dve.wait_ge(s_load, 16 * N_LOAD)
            if first:
                v_.memset(mean_w[:, :], 1.0 / D).then_inc(s_set, 1)
                v_.memset(eps_ln[:, :], EPS_LN).then_inc(s_set, 1)
                v_.memset(eps_scan[:, :], EPS_SCAN).then_inc(s_set, 1)
                v_.memset(one[:, :], 1.0).then_inc(s_set, 1)
                v_.tensor_copy(sel[:, :, :], rep32[:, :].unsqueeze(2).broadcast_to([3 * BC, BC, 128])).then_inc(s_set, 1)
                for m in range(DH):
                    v_.tensor_scalar(posb[:, m, 1:SEQ], pos[:, m, 1:SEQ], clsb[:, m, 1:2], None, ALU.add)
                    v_.tensor_scalar(posb[:, m, 0:1], pos[:, m, 0:1], clsb[:, m, 0:1], None,
                                     ALU.add).then_inc(s_set, 1)
                v_.memset(y[:, 0, 0:1], 0.0).then_inc(s_set, 1)
            for b in blocks:
                v_.tensor_scalar(b.a[:, :], b.vec[:, V_ALOG:V_COLS], LOG_RATE_MAX, None, ALU.min).then_inc(s_alog, 1)
            for b in blocks:
                dve.wait_ge(s_seta, NB)
                v_.tensor_scalar(b.a[:, :], b.a[:, :], -1.0, None, ALU.mult).then_inc(s_seta, 1)
            dve.wait_ge(s_zero, N_ZERO)
            since(dve, s_set, N_SETV)

            def cent(n, c, src):
                dve.wait_ge(n.s_mean, c + 1)
                v_.tensor_tensor(n.cent[:, :, :], src, ps[0:DP, 0:1, 0:CT].broadcast_to([DP, DH, CT]),
                                 ALU.subtract).then_inc(n.s_cent, 1)

            def norm_z(n, c):
                dve.wait_ge(n.s_rstd, c * 2 + 2)
                v_.tensor_tensor(n.z[:, :, :], n.cent[:, :, :], n.rstd[:, :].unsqueeze(1).broadcast_to([DP, DH, CT]),
                                 ALU.mult).then_inc(n.s_z, 1)

            def here(x):
                return h_all[:, :, bass.ds(x.c * CT, CT)]

            def f_tok(x):
                if not first:
                    return
                dve.wait_ge(s_tok, x.c + 1)
                for m in range(DH):
                    tokens = h_all[:, m, bass.ds(x.c * CT, CT)].rearrange("p (i t) -> p i t", t=SEQ)
                    v_.tensor_tensor(tokens[:, :, 1:SEQ],
                                     ps[0:DP, m, 0:CPATCH].rearrange("p (i t) -> p i t", t=PATCHES),
                                     posb[:, m:m + 1, 1:SEQ].broadcast_to([DP, CI, PATCHES]), ALU.add).then_inc(s_tokh, 1)
                tokens = here(x).rearrange("p m (i t) -> p m i t", t=SEQ)
                v_.tensor_copy(tokens[:, :, :, 0:1],
                               posb[:, :, 0:1].unsqueeze(2).broadcast_to([DP, DH, CI, 1])).then_inc(s_tokh, 1)

            def f_cent(x):
                if x.opens:
                    if first:
                        dve.wait_ge(s_tokh, x.c * 3 + 3)
                    cent(before, x.c, here(x))

            def f_z(x):
                if x.opens:
                    norm_z(before, x.c)

            def f_conv(x):
                b = x.b
                dve.wait_ge(s_xpad, x.u + 1)
                for k in range(TAPS):
                    for j in range(J):
                        at = TAPS - 1 - k if b.rev else k
                        src = b.xpad[:, j, :, at:at + SEQ]
                        o = imgs(conv[:, j, :])
                        if k == 0:
                            v_.tensor_scalar(o, src, b.conv_w(j, k), None, ALU.mult).then_inc(s_conv, 1)
                        else:
                            dve.wait_ge(s_conv, x.u * TAPS * J + (k - 1) * J + j + 1)
                            v_.scalar_tensor_tensor(o, src, b.conv_w(j, k), o, ALU.mult, ALU.add).then_inc(s_conv, 1)

            def f_parts(x):
                p = parts[x.buf]
                dve.wait_ge(s_dblc, x.u * 3 + 3)
                v_.tensor_tensor(bcr[:, :], bc[:, :], p[:, :], ALU.subtract).then_inc(s_parts, 1)
                dve.wait_ge(s_parts, x.u * 5 + 1)
                for lo in (BC, 2 * BC):
                    v_.tensor_copy(p[lo:lo + BC, :], bcr[lo:lo + BC, :]).then_inc(s_parts, 1)
                dve.wait_ge(s_parts, x.u * 5 + 3)
                last = slice(2 * BC, 3 * BC)
                v_.tensor_tensor(bcr[last, :], bcr[last, :], p[last, :], ALU.subtract).then_inc(s_parts, 1)
                dve.wait_ge(s_parts, x.u * 5 + 4)
                v_.tensor_copy(p[last, :], bcr[last, :]).then_inc(s_parts, 1)

            def f_delta(x):
                dve.wait_ge(s_exp, x.u * 2 + 1)
                if x.b.ratio:
                    pass
                since(dve, s_dec, x.u * (STATES * J))
                v_.tensor_scalar(delta[:, :, :], absx[:, :, :], 1.0, -1.0, ALU.add, ALU.add).then_inc(s_low, 1)
                dve.wait_ge(s_low, x.u * 2 + 1)
                v_.tensor_tensor(delta[:, :, :], absx[:, :, :], delta[:, :, :], ALU.subtract).then_inc(s_low, 1)
                dve.wait_ge(s_low, x.u * 2 + 2)
                dve.wait_ge(s_exp, x.u * 2 + 2)
                v_.scalar_tensor_tensor(delta[:, :, :], lnx[:, :, :], 0.0, delta[:, :, :], ALU.max,
                                        ALU.add).then_inc(s_delta, 1)
                dve.wait_ge(s_delta, x.u * 2 + 1)
                dve.wait_ge(s_abs, x.u * 2 * J + 2 * J)
                v_.tensor_tensor(delta[:, :, :], delta[:, :, :], relux[:, :, :], ALU.add).then_inc(s_delta, 1)
                dve.wait_ge(s_delta, x.u * 2 + 2)
                if x.b.ratio:
                    def back(ap):
                        return ap[:, ::-1]
                    v_.tensor_tensor_scan(back(suffix[:, :, :].rearrange("p j t -> p (j t)")),
                                          back(keep_bwd[:, :, :].rearrange("p i t -> p (i t)")),
                                          back(delta[:, :, :].rearrange("p j t -> p (j t)")), 0.0,
                                          ALU.mult, ALU.add).then_inc(s_suf, 1)
                v_.tensor_tensor(dx[:, :, :], delta[:, :, :], xc[x.buf][:, :, :], ALU.mult).then_inc(s_dx, 1)

            def flat(x, ap):
                f = ap[:, :, :, :].rearrange("p n j t -> p (n j t)")
                return f[:, ::-1] if x.b.rev else f

            def row(idx):
                return ps_bc[:, idx % 2:idx % 2 + 1, 0:CT].broadcast_to([128, J, CT])

            def b_products(x, gi):
                if gi == 0:
                    dve.wait_ge(s_dx, x.u + 1)
                since(dve, s_sum, x.g + gi - 1)
                for n in range(NS):
                    idx = b_row(gi, n)
                    dve.wait_ge(s_bc, x.u * (2 * STATES) + idx + 1)
                    v_.tensor_tensor(val[gi % 2][:, n, :, :], dx[:, :, :], row(idx), ALU.mult).then_inc(s_v, 1)

            def scan(x, gi):
                v = flat(x, val[gi % 2])
                gu = x.g + gi
                if x.b.ratio:
                    dve.wait_ge(s_ve, gu + 1)
                    keep_ = keep_fwd[:, :, :].rearrange("p i t -> p (i t)")
                    v_.tensor_tensor_scan(v, keep_, v, 0.0, ALU.mult, ALU.add).then_inc(s_scan, 1)
                    dve.wait_ge(s_scan, gu + 1)
                    dve.wait_ge(s_inv, gu * 2 + 2)
                    v_.tensor_tensor(v, v, flat(x, inv), ALU.mult).then_inc(s_vr, 1)
                else:
                    dve.wait_ge(s_v, x.u * STATES + (gi + 1) * NS)
                    dve.wait_ge(s_dec, (gu + 1) * (NS * J))
                    v_.tensor_tensor_scan(v, flat(x, x.b.decay[gi % 2]), v, 0.0, ALU.mult, ALU.add).then_inc(s_scan, 1)

            def c_products(x, gi):
                v = val[gi % 2]
                dve.wait_ge(s_vr if x.b.ratio else s_scan, x.g + gi + 1)
                for n in range(NS):
                    idx = c_row(gi, n)
                    dve.wait_ge(s_bc, x.u * (2 * STATES) + idx + 1)
                    v_.tensor_tensor(v[:, n, :, :], v[:, n, :, :], row(idx), ALU.mult).then_inc(s_hcm, 1)

            def t_y(x):
                dve.wait_ge(s_sum, x.g + NG)
                since(dve, s_out, x.u)
                for j in range(J):
                    v_.scalar_tensor_tensor(y[:, j, :], xc[x.buf][:, j, :], x.b.col(V_SKIP, j), ps_y[:, j, 0:CT],
                                            ALU.mult, ALU.add).then_inc(s_skip, 1)
                dve.wait_ge(s_skip, x.u * J + J)
                v_.tensor_tensor(y[:, :, :], y[:, :, :], gate[x.buf][:, :, :], ALU.mult).then_inc(s_y, 1)

            def t_hc(x):
                dve.wait_ge(s_out, x.u + 1)
                res = ps[0:DP, 0:DH, 0:CT]
                base = x.c * HC_PER
                if x.opens:
                    since(dve, s_chunk, 2 * x.c)
                    v_.tensor_tensor(hc[:, :, :], here(x), res, ALU.add).then_inc(s_hc, 1)
                    if not first:
                        dve.wait_ge(s_hc, base + 1)
                        v_.tensor_tensor(hc[:, :, :], hc[:, :, :], before.z[:, :, :], ALU.add).then_inc(s_hc, 1)
                else:
                    dve.wait_ge(s_hc, base + 2)
                    v_.tensor_tensor(hc[:, :, :], hc[:, :, :], res, ALU.add).then_inc(s_hc, 1)

            def t_cent(x):
                if x.ends:
                    dve.wait_ge(s_hc, x.c * HC_PER + HC_PER)
                    cent(behind, x.c, hc[:, :, :])

            def t_z(x):
                if x.ends:
                    if first:
                        since(dve, s_zst, 16 * x.c)
                    norm_z(behind, x.c)
                    v_.tensor_copy(here(x), hc[:, :, :]).then_inc(s_chunk, 1)

            def t_store(x):
                if x.ends:
                    dve.wait_ge(s_logit, x.c + 1)
                    v_.tensor_copy(logits_all[:, bass.ds(x.c * TG, TG), :],
                                   ps[0:TP, 2, 0:TG * LOGITS].rearrange("p (q e) -> p q e", e=LOGITS)).then_inc(s_chunk, 1)

            class Run:
                def front(self, f):
                    for step in (f_tok, f_cent, f_z, f_conv, f_parts, f_delta):
                        step(f)

                def main(self, x, tail, front):
                    def do(step, unit):
                        if unit is not None:
                            step(unit)

                    b_products(x, 0)
                    do(t_y, tail)
                    b_products(x, 1)
                    do(t_hc, tail)
                    scan(x, 0)
                    do(t_cent, tail)
                    c_products(x, 0)
                    do(t_z, tail)
                    b_products(x, 2)
                    do(t_store, tail)
                    scan(x, 1)
                    do(f_tok, front)
                    c_products(x, 1)
                    do(f_cent, front)
                    b_products(x, 3)
                    do(f_z, front)
                    scan(x, 2)
                    do(f_conv, front)
                    c_products(x, 2)
                    scan(x, 3)
                    c_products(x, 3)
                    do(f_parts, front)
                    do(f_delta, front)

                def last(self, x):
                    for step in (t_y, t_hc, t_cent, t_z, t_store):
                        step(x)

            units(dve, Run())


def expert_phase(nc, t, h_all, route_all, ident, sel):
    with ExitStack() as ctx:
        def sb(name, shape, dt):
            return ctx.enter_context(nc.sbuf_tensor(f"b_{name}", shape, dt))

        def pb(name, shape, dt):
            return ctx.enter_context(nc.psum_tensor(f"b_{name}", shape, dt))

        def sem(name):
            return ctx.enter_context(nc.semaphore(f"b_{name}"))

        z_all = sb("z_all", [DP, DH, TOKENS], F32)
        w_gate = [sb(f"w_gate{i}", [DP, DH, HID], F32) for i in range(2)]
        w_up = [sb(f"w_up{i}", [DP, DH, HID], F32) for i in range(2)]
        w_down = [sb(f"w_down{i}", [128, HK, D], F32) for i in range(2)]
        order = sb("order", [TP, EXPERTS], F32)
        best = sb("best", [TP, 2, GROUPS], F32)
        first = sb("first", [TP, GROUPS], F32)
        hit = sb("hit", [TP, GROUPS, EXPERTS], F32)
        pick = [sb(f"pick{i}", [TP, GROUPS, EXPERTS], F32) for i in range(2)]
        rest = sb("rest", [TP, GROUPS, EXPERTS], F32)
        gap = sb("gap", [TP, GROUPS], F32)
        ex = sb("ex", [TP, GROUPS], F32)
        den = sb("den", [TP, GROUPS], F32)
        share = [sb(f"share{i}", [TP, GROUPS], F32) for i in range(2)]
        weight = sb("weight", [TP, GROUPS, EXPERTS], F32)
        left = sb("left", [TP, GROUPS, EXPERTS], F32)
        wparts = sb("wparts", [TP, GROUPS, 3 * BC], BF16)
        identb = sb("identb", [128, 128], BF16)
        wt = sb("wt", [3 * BC, TOKENS], BF16)
        wrow = [sb(f"wrow{i}", [DP, CT], F32) for i in range(2)]
        act_g = [sb(f"act_g{i}", [128, CT], F32) for i in range(2)]
        hid = [sb(f"hid{i}", [128, HK, CT], F32) for i in range(2)]
        scaled = [sb(f"scaled{i}", [DP, DH, CT], F32) for i in range(2)]

        ps_gu = [pb(f"ps_gu{i}", [128, 2, BANK], F32) for i in range(2)]
        ps_w = pb("ps_w", [128, BANK], F32)
        ps_t = pb("ps_t", [128, 2 * BANK], BF16)
        ps_d = pb("ps_d", [128, DH, BANK], F32)

        s_w = [sem(f"s_w{i}") for i in range(2)]
        s_zl = sem("s_zl")
        s_order = sem("s_order")
        s_r = sem("s_r")
        s_ex = sem("s_ex")
        s_t = sem("s_t")
        s_tc = sem("s_tc")
        s_row = sem("s_row")
        s_rowc = sem("s_rowc")
        s_gu = sem("s_gu")
        s_act = sem("s_act")
        s_hid = sem("s_hid")
        s_d = sem("s_d")
        s_sc = sem("s_sc")
        s_acc = sem("s_acc")
        block = ctx.enter_context(nc.Block())
        PAIRS = EXPERTS // 2

        @block.sync
        def _(sp):
            def load(i, e):
                sp.dma_start(w_gate[i][:, :, :], t["w_gate"][e]).then_inc(s_w[i], 16)
                sp.dma_start(w_up[i][:, :, :], t["w_up"][e]).then_inc(s_w[i], 16)
                sp.dma_start(w_down[i][:, :, :], t["w_down"][e]).then_inc(s_w[i], 16)
            sp.dma_start(z_all[:, :, :], t["z_scratch"]).then_inc(s_zl, 16)
            load(0, 0)
            load(1, 1)
            with sp.Fori(0, PAIRS - 1) as pair:
                for i in range(2):
                    sp.wait_ge(s_d, (pair * 2 + i + 1) * CHUNKS)
                    load(i, pair * 2 + 2 + i)

        @block.gpsimd
        def _(pool):
            g = nc.gpsimd
            for e in range(EXPERTS):
                g.memset(order[:, e:e + 1], float(e - EXPERTS)).then_inc(s_order, 1)
            g.memset(wparts[:, :, :], 0.0).then_inc(s_order, 1)
            pool.sem_inc(s_acc, 1)
            with pool.Fori(0, EXPERTS) as e:
                with pool.Fori(0, CHUNKS // 2) as cp:
                    for i in range(2):
                        s = e * CHUNKS + cp * 2 + i
                        pool.wait_ge(s_sc, s + 1 + 1)
                        here = bass.ds((cp * 2 + i) * CT, CT)
                        pool.wait_ge(s_acc, s + 1)
                        g.tensor_tensor(h_all[:, :, here], h_all[:, :, here], scaled[i][:, :, :],
                                        ALU.add).then_inc(s_acc, 1)

        @block.vector
        def _(dve):
            v_ = nc.vector
            dve.wait_ge(s_order, EXPERTS + 1)
            for s in (s_sc, s_hid, s_tc):
                dve.sem_inc(s, 1)
            steps = [0]

            def step(ins):
                steps[0] += 1
                ins.then_inc(s_r, 1)
                dve.wait_ge(s_r, steps[0])

            def wide(ap):
                return ap.unsqueeze(2).broadcast_to([TP, GROUPS, EXPERTS])

            ord_b = order[:, :].unsqueeze(1).broadcast_to([TP, GROUPS, EXPERTS])
            step(v_.tensor_copy(identb[:, :], ident[:, :]))
            logit = route_all
            for i in range(2):
                top = best[:, i, :]
                step(v_.tensor_reduce(top, logit[:, :, :], AX_X, ALU.max))
                step(v_.tensor_tensor(hit[:, :, :], logit[:, :, :], wide(top), ALU.is_equal))
                step(v_.tensor_tensor(hit[:, :, :], hit[:, :, :], ord_b, ALU.mult))
                step(v_.tensor_reduce(first[:, :], hit[:, :, :], AX_X, ALU.min))
                step(v_.tensor_tensor(pick[i][:, :, :], wide(first[:, :]), ord_b, ALU.is_equal))
                if i == 0:
                    step(v_.scalar_tensor_tensor(rest[:, :, :], pick[0][:, :, :], -3.0e38, logit[:, :, :],
                                                 ALU.mult, ALU.add))
                    logit = rest
            step(v_.tensor_tensor(gap[:, :], best[:, 1, :], best[:, 0, :], ALU.subtract))
            dve.wait_ge(s_ex, 1)
            step(v_.tensor_scalar(den[:, :], ex[:, :], 1.0, None, ALU.add))
            step(v_.reciprocal(share[0][:, :], den[:, :]))
            step(v_.tensor_tensor(share[1][:, :], share[0][:, :], ex[:, :], ALU.mult))
            step(v_.tensor_tensor(weight[:, :, :], pick[0][:, :, :], wide(share[0][:, :]), ALU.mult))
            step(v_.tensor_tensor(left[:, :, :], pick[1][:, :, :], wide(share[1][:, :]), ALU.mult))
            step(v_.tensor_tensor(weight[:, :, :], weight[:, :, :], left[:, :, :], ALU.add))
            src = weight
            for i in range(3):
                step(v_.tensor_copy(wparts[:, :, i * BC:i * BC + EXPERTS], src[:, :, :]))
                if i < 2:
                    step(v_.tensor_tensor(left[:, :, :], src[:, :, :], wparts[:, :, i * BC:i * BC + EXPERTS],
                                          ALU.subtract))
                    src = left
            assert steps[0] == ROUTE_STEPS
            with dve.Fori(0, CHUNKS) as c:
                dve.wait_ge(s_t, c + 1)
                v_.tensor_copy(wt[:, bass.ds(c * CT, CT)], ps_t[0:3 * BC, 0:CT]).then_inc(s_tc, 1)
            with dve.Fori(0, EXPERTS) as e:
                with dve.Fori(0, CHUNKS // 2) as cp:
                    for i in range(2):
                        s = e * CHUNKS + cp * 2 + i
                        for k in range(HK):
                            dve.wait_ge(s_act, s * HK + k + 1)
                            v_.tensor_tensor(hid[i][:, k, :], act_g[k % 2][:, :], ps_gu[k % 2][:, 1, 0:CT],
                                             ALU.mult).then_inc(s_hid, 1)
                        dve.wait_ge(s_d, s + 1)
                        dve.wait_ge(s_rowc, s + 1 + 1)
                        dve.wait_ge(s_acc, e * CHUNKS + cp * 2 + 1)
                        v_.tensor_tensor(scaled[i][:, :, :], ps_d[0:DP, :, 0:CT],
                                         wrow[i][:, :].unsqueeze(1).broadcast_to([DP, DH, CT]),
                                         ALU.mult).then_inc(s_sc, 1)

        @block.scalar
        def _(act):
            a = nc.scalar.activation
            act.wait_ge(s_r, GAP_STEP)
            a(ex[:, :], gap[:, :], ACT.Exp).then_inc(s_ex, 1)
            act.sem_inc(s_rowc, 1)
            with act.Fori(0, EXPERTS) as e:
                with act.Fori(0, CHUNKS // 2) as cp:
                    for i in range(2):
                        s = e * CHUNKS + cp * 2 + i
                        act.wait_ge(s_row, s + 1)
                        act.wait_ge(s_sc, e * CHUNKS + cp * 2 + 1)
                        a(wrow[i][:, :], ps_w[0:DP, 0:CT], ACT.Copy).then_inc(s_rowc, 1)
                        for k in range(HK):
                            act.wait_ge(s_gu, s * HK + k + 1)
                            act.wait_ge(s_hid, s * HK + max(k - 1, 0) + 1)
                            a(act_g[k % 2][:, :], ps_gu[k % 2][:, 0, 0:CT], ACT.Silu).then_inc(s_act, 1)

        @block.tensor
        def _(pe):
            mm = nc.tensor.matmul
            pe.wait_ge(s_r, ROUTE_STEPS)
            with pe.Fori(0, CHUNKS) as c:
                pe.wait_ge(s_tc, c + 1)
                for q in range(TG):
                    m = nc.tensor.transpose(ps_t[0:3 * BC, q * TP:(q + 1) * TP],
                                            wparts[:, bass.ds(c * TG + q, 1), :].rearrange("p a k -> p (a k)"),
                                            identb[0:TP, 0:TP])
                m.then_inc(s_t, 1)
            pe.wait_ge(s_tc, CHUNKS + 1)
            pe.wait_ge(s_zl, 16)
            with pe.Fori(0, PAIRS) as pair:
                for wi in range(2):
                    with pe.Fori(0, CHUNKS // 2) as cp:
                        for i in range(2):
                            c = cp * 2 + i
                            s = (pair * 2 + wi) * CHUNKS + c
                            here = bass.ds(c * CT, CT)
                            pe.wait_ge(s_w[wi], pair * 48 + 48)
                            pe.wait_ge(s_rowc, s + 1)
                            mm(ps_w[:, 0:CT], sel_row(sel, wi, pair), wt[:, here], start=True,
                               stop=True).then_inc(s_row, 1)
                            for k in range(HK):
                                pe.wait_ge(s_hid, s * HK + max(k - 1, 0) + 1)
                                for g_, w in enumerate((w_gate[wi], w_up[wi])):
                                    for kk in range(DH):
                                        m = mm(ps_gu[k % 2][:, g_, 0:CT], w[:, kk, k * 128:(k + 1) * 128],
                                               z_all[:, kk, here], start=(kk == 0), stop=(kk == DH - 1))
                                m.then_inc(s_gu, 1)
                            pe.wait_ge(s_hid, s * HK + HK + 1)
                            pe.wait_ge(s_sc, s + 1)
                            for m_ in range(DH):
                                for k in range(HK):
                                    m = mm(ps_d[0:DP, m_, 0:CT], w_down[wi][:, k, m_ * DP:(m_ + 1) * DP], hid[i][:, k, :],
                                           start=(k == 0), stop=(k == HK - 1))
                            m.then_inc(s_d, 1)


ROUTE_STEPS = 1 + 5 + 1 + 5 + 1 + 3 + 3 + 5
GAP_STEP = 13


def sel_row(sel, wi, pair):
    return sel[:, bass.ds(pair * 2 + wi, 1), :].rearrange("p a k -> p (a k)")


def tree_phase(nc, t, h_all, node_all, ident):
    with ExitStack() as ctx:
        def sb(name, shape, dt):
            return ctx.enter_context(nc.sbuf_tensor(f"d_{name}", shape, dt))

        def pb(name, shape, dt):
            return ctx.enter_context(nc.psum_tensor(f"d_{name}", shape, dt))

        def sem(name):
            return ctx.enter_context(nc.semaphore(f"d_{name}"))

        w_node = sb("w_node", [NODES, D], F32)
        gelu = sb("gelu", [TP, GROUPS, NODES], F32)
        right_ = sb("right", [TP, GROUPS, NODES], F32)
        reach = sb("reach", [TP, GROUPS, NODES], F32)
        passed = sb("passed", [TP, GROUPS, NODES], F32)
        coef = sb("coef", [TP, GROUPS, NODES], F32)
        turn = sb("turn", [TP, GROUPS, NODES], F32)
        coef_c = [sb(f"coef_c{i}", [TP, TG, NODES], F32) for i in range(2)]
        red = sb("red", [TP, GROUPS], F32)
        red2 = sb("red2", [TP, GROUPS], F32)
        coef_t = [sb(f"coef_t{i}", [NODES, CT], F32) for i in range(2)]
        outc = [sb(f"outc{i}", [DP, DH, CT], F32) for i in range(2)]
        ps_t = [pb(f"ps_t{i}", [128, BANK], F32) for i in range(2)]
        ps_o = [pb(f"ps_o{i}", [128, DH, BANK], F32) for i in range(2)]
        s_w = sem("s_w")
        s_g = sem("s_g")
        s_s = sem("s_s")
        s_cc = sem("s_cc")
        s_t = sem("s_t")
        s_tc = sem("s_tc")
        s_o = sem("s_o")
        s_oc = sem("s_oc")
        s_st = sem("s_st")
        block = ctx.enter_context(nc.Block())
        FIRST_LEAF = 15
        LAST = NODES - 1

        @block.sync
        def _(sp):
            sp.dma_start(w_node[:, :], t["node_out"]).then_inc(s_w, 16)
            sp.sem_inc(s_st, 1)
            with sp.Fori(0, CHUNKS // 2) as cp:
                for i in range(2):
                    sp.wait_ge(s_oc, cp * 2 + i + 1 + 1)
                    sp.dma_start(t["out"][cp * 2 + i], outc[i][:, :, :]).then_inc(s_st, 16)
            sp.wait_ge(s_st, 16 * CHUNKS + 1)

        @block.scalar
        def _(act):
            nc.scalar.activation(gelu[:, :, :], node_all[:, :, :], ACT.Gelu).then_inc(s_g, 1)

        @block.vector
        def _(dve):
            v_ = nc.vector
            steps = [0]

            def step(ins):
                steps[0] += 1
                ins.then_inc(s_s, 1)
                dve.wait_ge(s_s, steps[0])

            tt = v_.tensor_tensor
            step(v_.tensor_scalar(right_[:, :, :], node_all[:, :, :], 0.0, None, ALU.is_gt))
            step(v_.memset(reach[:, :, :], 0.0))
            step(v_.memset(reach[:, :, 0:1], 1.0))

            def children(ap, lo, n):
                c = ap[:, :, 2 * lo + 1:2 * lo + 1 + 2 * n].rearrange("p g (n s) -> p g n s", s=2)
                return c[:, :, :, 0], c[:, :, :, 1]

            for lo, n in ((0, 1), (1, 2), (3, 4), (7, 3)):
                left, right = children(reach, lo, n)
                here = slice(lo, lo + n)
                step(tt(turn[:, :, here], reach[:, :, here], right_[:, :, here], ALU.mult))
                step(v_.tensor_copy(right, turn[:, :, here]))
                step(tt(left, reach[:, :, here], turn[:, :, here], ALU.subtract))
            step(v_.tensor_reduce(red[:, :], reach[:, :, 10:FIRST_LEAF], AX_X, ALU.add))
            last = reach[:, :, LAST:NODES].rearrange("p g a -> p (g a)")
            dve.wait_ge(s_g, 1)
            step(tt(passed[:, :, 0:LAST], reach[:, :, 0:LAST], gelu[:, :, 0:LAST], ALU.mult))
            for lo, n in ((0, 1), (1, 2), (3, 4), (7, 3)):
                for child, out in zip(children(reach, lo, n), children(coef, lo, n)):
                    step(tt(out, child, gelu[:, :, lo:lo + n], ALU.mult))
            step(v_.memset(coef[:, :, 0:1], 0.0))
            step(tt(last, last, red[:, :], ALU.add))
            step(v_.tensor_reduce(red[:, :], passed[:, :, 10:LAST], AX_X, ALU.add))
            own = gelu[:, :, LAST:NODES].rearrange("p g a -> p (g a)")
            cl = coef[:, :, LAST:NODES].rearrange("p g a -> p (g a)")
            step(tt(red2[:, :], last, own, ALU.mult))
            step(tt(cl, cl, red[:, :], ALU.add))
            step(tt(cl, cl, red2[:, :], ALU.add))
            step(v_.scalar_tensor_tensor(cl, own, float(FFF_STEPS - 5), cl, ALU.mult, ALU.add))
            assert steps[0] == TREE_STEPS
            dve.sem_inc(s_oc, 1)
            with dve.Fori(0, CHUNKS // 2) as cp:
                for i in range(2):
                    c = cp * 2 + i
                    v_.tensor_copy(coef_c[i][:, :, :], coef[:, bass.ds(c * TG, TG), :]).then_inc(s_cc, 1)
                    dve.wait_ge(s_t, c + 1)
                    v_.tensor_copy(coef_t[i][:, :], ps_t[i][0:NODES, 0:CT]).then_inc(s_tc, 1)
                    dve.wait_ge(s_o, c + 1)
                    dve.wait_ge(s_st, cp * 32 + 1)
                    v_.tensor_tensor(outc[i][:, :, :], h_all[:, :, bass.ds(c * CT, CT)], ps_o[i][0:DP, :, 0:CT],
                                     ALU.add).then_inc(s_oc, 1)

        @block.tensor
        def _(pe):
            mm = nc.tensor.matmul
            pe.wait_ge(s_w, 16)
            pe.wait_ge(s_s, TREE_STEPS)
            with pe.Fori(0, CHUNKS // 2) as cp:
                for i in range(2):
                    c = cp * 2 + i
                    pe.wait_ge(s_cc, c + 1)
                    for q in range(TG):
                        m = nc.tensor.transpose(ps_t[i][0:NODES, q * TP:(q + 1) * TP],
                                                coef_c[i][:, q, :],
                                                ident[0:TP, 0:TP])
                    m.then_inc(s_t, 1)
                    pe.wait_ge(s_tc, c + 1)
                    pe.wait_ge(s_oc, c + 1)
                    for m_ in range(DH):
                        m = mm(ps_o[i][0:DP, m_, 0:CT], w_node[:, m_ * DP:(m_ + 1) * DP], coef_t[i][:, :],
                               start=True, stop=True)
                    m.then_inc(s_o, 1)


TREE_STEPS = 3 + 12 + 1 + 1 + 8 + 2 + 1 + 4


def kernel(**inputs):
    import concourse.bacc as _bacc
    from concourse.bass_utils import run_bass_kernel_spmd as _run

    a = {k: np.ascontiguousarray(v) for k, v in inputs.items()}
    cont = np.ascontiguousarray

    def halves(w):
        return w.reshape(DH, DP, -1).transpose(1, 0, 2)

    def tiles(w):
        return w.reshape(-1, 128, w.shape[-1]).transpose(1, 0, 2)

    def mamba(w_in, conv_w, conv_b, w_x, w_dt, b_dt, a_log, skip, w_out):
        rank = w_dt.shape[0]
        bc = w_x[:, rank:]
        vec = [tiles(conv_w.reshape(INNER, TAPS)).reshape(128, -1)]
        vec += [tiles(v.reshape(INNER, 1)).reshape(128, -1) for v in (conv_b, b_dt, skip)]
        vec += [tiles(a_log).reshape(128, -1)]
        return [halves(w_in), tiles(np.concatenate([w_x, bc, bc], axis=1)), w_dt, tiles(w_out),
                np.concatenate(vec, axis=1)]

    x = a["x"].reshape(CHUNKS, CI, COLORS, GRID, PATCH, GRID, PATCH)
    x = x.transpose(0, 2, 4, 6, 1, 3, 5).reshape(CHUNKS, PK, 128, CPATCH).transpose(0, 2, 1, 3)
    arrays = {
        "x": x,
        "w_tok": tiles(a["L0_tok_W"].T),
        "pos": halves(a["L0_tok_position_embed"].reshape(SEQ, D).T),
        "clsb": halves(np.stack([a["L0_tok_class_embed"].reshape(D), a["L0_tok_b"]], axis=1)),
        "router": halves(a["L0_ffn_router_w"].T),
        "w_gate": a["L0_ffn_Wg"].reshape(EXPERTS, HID, DH, DP).transpose(0, 3, 2, 1),
        "w_up": a["L0_ffn_Wu"].reshape(EXPERTS, HID, DH, DP).transpose(0, 3, 2, 1),
        "w_down": a["L0_ffn_Wd"].reshape(EXPERTS, D, HK, 128).transpose(0, 3, 2, 1),
        "node_in": halves(a["L1_ffn_weights_in"].T),
        "node_out": a["L1_ffn_weights_out"],
        "ident": np.eye(128, dtype=np.float32),
        "rep32": np.tile(np.eye(BC, dtype=np.float32), (3, 1)),
    }
    packed = {"m0": mamba(*(a["L0_attn_" + k] for k in ("W_in", "conv_w", "conv_b", "W_x", "W_dt", "b_dt", "A_log",
                                                        "Dp", "W_out")))}
    for name, d in (("mf", "fwd"), ("mb", "bwd")):
        g = {k: a[f"L1_attn_{d}_{k}"] for k in ("W_in", "conv_w", "conv_b", "W_x", "W_dt", "b_dt", "A_log", "D", "W_out")}
        packed[name] = mamba(g["W_in"].T, g["conv_w"], g["conv_b"], g["W_x"].T, g["W_dt"].T, g["b_dt"], g["A_log"],
                             g["D"], g["W_out"].T)

    nc = _bacc.Bacc("TRN2", target_bir_lowering=False, num_devices=1)
    feed, t = {}, {}

    def given(name, value):
        feed[name] = cont(value)
        return nc.dram_tensor(name, feed[name].shape, F32, kind="ExternalInput").ap()

    for name, value in arrays.items():
        t[name] = given("in_" + name, value)
    for name, values in packed.items():
        t[name] = [given(f"in_{name}_{i}", v) for i, v in enumerate(values)]
    t["z_scratch"] = nc.dram_tensor("z_scratch", (DP, DH, TOKENS), F32, kind="Internal").ap()
    t["out"] = nc.dram_tensor("out_0", (CHUNKS, DP, DH, CT), F32, kind="ExternalOutput").ap()
    build(nc, t)
    r = _run(nc, [feed], core_ids=[0])
    out = r.results[0]["out_0"].reshape(CHUNKS, DP, DH, CI, SEQ)
    return cont(out.transpose(0, 3, 4, 2, 1).reshape(IMAGES, SEQ, D))
```
